# Optimizing a Trainium2 kernel written in Bass

```python
import numpy as np
import jax
import jax.numpy as jnp

def _softmax(x, axis=-1):
    return jax.nn.softmax(x, axis=axis)
def _gelu(x):
    return jax.nn.gelu(x, approximate=True)
def _silu(x):
    return jax.nn.silu(x)
def _sigmoid(x):
    return jax.nn.sigmoid(x)
def _layernorm(x, axis=-1, eps=1e-5):
    m = jnp.mean(x, axis=axis, keepdims=True)
    v = jnp.var(x, axis=axis, keepdims=True)
    return (x - m) / jnp.sqrt(v + eps)
def _scatter_add(tgt, idx, src, axis=0):
    return tgt.at[idx].add(src)
def _segment_sum(src, seg, n):
    return jax.ops.segment_sum(src, seg, n)

kernel_name = 'mk_conv_seq_d1_conv_nchw256_124839'

def setup_inputs(seed: int = 0):
    np.random.seed(seed)
    _w = jnp.asarray
    def _rec_inputs():
        import jax
        import jax.numpy as jnp
        _gk = jax.random.key(seed)
        x = 7.22e-05 + 1 * jax.random.normal(jax.random.fold_in(_gk, 1), (32, 256, 32, 32), jnp.float32)
        return x
    x = _rec_inputs()
    def _L0_conv_setup():
        import jax, jax.numpy as jnp
        import numpy as np
        EPS = 1e-05
        GROUPS = 8

        def group_norm(x, w, b):
            B, C, H, W = x.shape
            xg = x.reshape(B, GROUPS, C // GROUPS, H, W)
            mu = xg.mean(axis=(2, 3, 4), keepdims=True)
            var = xg.var(axis=(2, 3, 4), keepdims=True)
            xn = ((xg - mu) * jax.lax.rsqrt(var + EPS)).reshape(B, C, H, W)
            return xn * w[None, :, None, None] + b[None, :, None, None]
        key = jax.random.key(seed)
        ks = jax.random.split(key, 6)
        B, C, H, W = (32, 256, 32, 32)
        x = jax.random.normal(ks[0], (B, C, H, W), dtype=jnp.float32)
        norm_w = jnp.ones((C,), dtype=jnp.float32)
        norm_b = jnp.zeros((C,), dtype=jnp.float32)
        qkv_w = jax.random.normal(ks[1], (3 * C, C), dtype=jnp.float32) * C ** (-0.5)
        proj_w = jax.random.normal(ks[2], (C, C), dtype=jnp.float32) * C ** (-0.5)
        proj_b = jnp.zeros((C,), dtype=jnp.float32)
        return {'x': x, 'norm_w': norm_w, 'norm_b': norm_b, 'qkv_w': qkv_w, 'proj_w': proj_w, 'proj_b': proj_b}
    _L0_conv_all = _L0_conv_setup()
    _L0_conv_in = {k: v for k, v in _L0_conv_all.items() if k in ('norm_w', 'norm_b', 'qkv_w', 'proj_w', 'proj_b', )}
    del _L0_conv_all

    return {
        "x": x,
        "L0_conv_norm_w": _L0_conv_in["norm_w"],
        "L0_conv_norm_b": _L0_conv_in["norm_b"],
        "L0_conv_qkv_w": _L0_conv_in["qkv_w"],
        "L0_conv_proj_w": _L0_conv_in["proj_w"],
        "L0_conv_proj_b": _L0_conv_in["proj_b"],
    }

def reference(x, L0_conv_norm_w, L0_conv_norm_b, L0_conv_qkv_w, L0_conv_proj_w, L0_conv_proj_b):
    import jax
    import jax.numpy as jnp
    def _L0_conv_ref(x, norm_w, norm_b, qkv_w, proj_w, proj_b):
        import jax, jax.numpy as jnp
        import numpy as np
        EPS = 1e-05
        GROUPS = 8

        def group_norm(x, w, b):
            B, C, H, W = x.shape
            xg = x.reshape(B, GROUPS, C // GROUPS, H, W)
            mu = xg.mean(axis=(2, 3, 4), keepdims=True)
            var = xg.var(axis=(2, 3, 4), keepdims=True)
            xn = ((xg - mu) * jax.lax.rsqrt(var + EPS)).reshape(B, C, H, W)
            return xn * w[None, :, None, None] + b[None, :, None, None]
        B, C, H, W = x.shape
        N = H * W
        h = group_norm(x, norm_w, norm_b)
        qkv = jnp.einsum('oc,bchw->bohw', qkv_w, h)
        q, k, v = jnp.split(qkv, 3, axis=1)
        q = q.reshape(B, C, N).transpose(0, 2, 1)
        k = k.reshape(B, C, N)
        v = v.reshape(B, C, N).transpose(0, 2, 1)
        attn = jnp.einsum('bnc,bcm->bnm', q, k) * C ** (-0.5)
        attn = jax.nn.softmax(attn, axis=-1)
        out = jnp.einsum('bnm,bmc->bnc', attn, v)
        out = out.transpose(0, 2, 1).reshape(B, C, H, W)
        proj = jnp.einsum('oc,bchw->bohw', proj_w, out) + proj_b[None, :, None, None]
        return x + proj

    def _gn(v, G=32, eps=1e-5):
        B_, C_, H_, W_ = v.shape
        g = v.reshape(B_, G, C_ // G, H_, W_)
        m = jnp.mean(g, axis=(2, 3, 4), keepdims=True)
        s = jnp.var(g, axis=(2, 3, 4), keepdims=True)
        return ((g - m) / jnp.sqrt(s + eps)).reshape(v.shape)

    def _ln_c(v, eps=1e-6):
        m = jnp.mean(v, axis=1, keepdims=True)
        s = jnp.var(v, axis=1, keepdims=True)
        return (v - m) / jnp.sqrt(s + eps)

    def _ln_t(v, eps=1e-5):
        m = jnp.mean(v, axis=-1, keepdims=True)
        s = jnp.var(v, axis=-1, keepdims=True)
        return (v - m) / jnp.sqrt(s + eps)

    def _to_tokens(v):
        B_, C_, H_, W_ = v.shape
        return v.reshape(B_, C_, H_ * W_).transpose(0, 2, 1)
    def _from_tokens(t, like):
        B_, C_, H_, W_ = like.shape
        return t.transpose(0, 2, 1).reshape(B_, C_, H_, W_)

    x = _L0_conv_ref(x, L0_conv_norm_w, L0_conv_norm_b, L0_conv_qkv_w, L0_conv_proj_w, L0_conv_proj_b)
    return x


_drawn_inputs = setup_inputs


def setup_inputs(seed=0):
    import zlib

    import numpy as np

    out = dict(_drawn_inputs(seed))
    spreads = {'L0_conv_norm_w': (1.0, 0.2), 'L0_conv_norm_b': (0.0, 0.1), 'L0_conv_proj_b': (0.0, 0.1)}
    factors = {}
    for name, (base, spread) in spreads.items():
        noise = np.random.default_rng([zlib.crc32(name.encode()), seed]).standard_normal(out[name].shape)
        drawn = base * np.exp(spread * noise) if base else spread * noise
        out[name] = jnp.asarray(drawn.astype(out[name].dtype))
    for name, factor in factors.items():
        out[name] = (out[name] * factor).astype(out[name].dtype)
    return out
```

```python
from contextlib import ExitStack

import concourse.bass as bass
from concourse import mybir

ALU = mybir.AluOpType
ACT = mybir.ActivationFunctionType
AX_X = mybir.AxisListType.X
F32 = mybir.dt.float32
F32R = mybir.dt.float32r

P = 128
GROUPS = 8
EPS = 1e-5
DMA_INC = 16
BANK = 512
STEPS = 8
PV_LAG = 5


def positive(count):
    return not isinstance(count, int) or count > 0


def within(value, end):
    return not isinstance(value, int) or 0 <= value < end


def attention_block(nc, x, norm_w, norm_b, qkv_w, proj_w, proj_b, out):
    B, C, N = x.shape
    CT = C // P
    KB = N // P
    HALVES = N // BANK
    QB = BANK // P
    SCALE = float(C) ** -0.5
    GROUP = C // GROUPS
    OT = 3 * C // P
    LAST = B * STEPS
    assert KB == STEPS and HALVES == 2 and CT == 2 and P % GROUP == 0 and B % 2 == 0

    x_v = x.rearrange("b (t p) n -> b p t n", p=P)
    x_half = x.rearrange("b (t p) (h n) -> b h p t n", p=P, h=HALVES)
    out_half = out.rearrange("b (t p) (h n) -> b h p t n", p=P, h=HALVES)

    with ExitStack() as ctx:
        def sb(name, shape, dt=F32):
            return ctx.enter_context(nc.sbuf_tensor(name, shape, dt))

        def ps(name, shape):
            return ctx.enter_context(nc.psum_tensor(name, shape, F32))

        def sem(name):
            return ctx.enter_context(nc.semaphore(name))

        qkv_rows = sb("qkv_rows", [P, OT, C])
        proj_rows = sb("proj_rows", [P, CT, C])
        projT = sb("projT", [P, CT, C])
        mixw_hi = sb("mixw_hi", [P, CT, C], F32R)
        mixw_lo = sb("mixw_lo", [P, CT, C], F32R)
        valw_hi = sb("valw_hi", [P, CT, C], F32R)
        valw_lo = sb("valw_lo", [P, CT, C], F32R)
        gain_w = sb("gain_w", [P, CT])
        gain_b = sb("gain_b", [P, CT])
        out_b = sb("out_b", [P, CT])
        ident = sb("ident", [P, P])
        group_mean = sb("group_mean", [P, P])
        minus_half = sb("minus_half", [P, CT])

        x_sb = sb("x_sb", [P, 2, CT, N])
        bn = sb("bn", [P, CT, HALVES, 6])
        chan = sb("chan", [P, CT, 2])
        mu = sb("mu", [P, 2, CT])
        dev = sb("dev", [P, CT])
        dev2 = sb("dev2", [P, CT])
        spread = sb("spread", [P, CT])
        var_eps = sb("var_eps", [P, CT])
        rstd = sb("rstd", [P, CT])
        gain = sb("gain", [P, CT])
        h_hi = sb("h_hi", [P, 2, CT, N], F32R)
        h_lo = sb("h_lo", [P, 2, CT, N], F32R)

        mix_hi = sb("mix_hi", [P, CT, N], F32R)
        mix_lo = sb("mix_lo", [P, CT, N], F32R)
        val_hi = sb("val_hi", [P, KB, C], F32R)
        val_lo = sb("val_lo", [P, KB, C], F32R)
        neg_max = sb("neg_max", [P, 2])
        row_sum = sb("row_sum", [P, 2])
        row_inv = sb("row_inv", [P, 2])
        probs = sb("probs", [P, 2, N])
        pT_hi = sb("pT_hi", [P, HALVES, KB, BANK], F32R)
        pT_lo = sb("pT_lo", [P, HALVES, KB, BANK], F32R)
        y = sb("y", [P, HALVES, CT, BANK])

        ps_scores = ps("ps_scores", [P, N])
        ps_turn = ps("ps_turn", [P, KB, P])
        ps_task = ps("ps_task", [P, 2, BANK])
        ps_out = ps("ps_out", [P, CT, BANK])

        qkv_loaded = sem("qkv_loaded")
        proj_loaded = sem("proj_loaded")
        vectors_loaded = sem("vectors_loaded")
        x_loaded = [sem("x_loaded_even"), sem("x_loaded_odd")]
        again_loaded = [sem("again_loaded_0"), sem("again_loaded_1")]
        stored = [sem("stored_0"), sem("stored_1")]
        zeroed = sem("zeroed")
        ident_ready = sem("ident_ready")
        half_ready = sem("half_ready")
        mean_zeroed = sem("mean_zeroed")
        const_ready = sem("const_ready")
        projT_done = sem("projT_done")
        projT_ready = sem("projT_ready")
        mixw_done = sem("mixw_done")
        valw_done = sem("valw_done")
        fold_hi = sem("fold_hi")
        fold_lo = sem("fold_lo")
        bn_ready = sem("bn_ready")
        chan_ready = sem("chan_ready")
        mean_done = sem("mean_done")
        dev_ready = sem("dev_ready")
        dev2_ready = sem("dev2_ready")
        spread_ready = sem("spread_ready")
        var_done = sem("var_done")
        var_ready = sem("var_ready")
        rstd_ready = sem("rstd_ready")
        gain_ready = sem("gain_ready")
        centred = sem("centred")
        h_hi_ready = sem("h_hi_ready")
        h_full = sem("h_full")
        h_ready = sem("h_ready")
        task_done = sem("task_done")
        task_hi = sem("task_hi")
        task_lo = sem("task_lo")
        scores_done = sem("scores_done")
        max_ready = sem("max_ready")
        exp_done = sem("exp_done")
        inv_ready = sem("inv_ready")
        probs_ready = sem("probs_ready")
        turn_done = sem("turn_done")
        pT_hi_ready = sem("pT_hi_ready")
        pT_lo_ready = sem("pT_lo_ready")
        pv_done = sem("pv_done")
        y_ready = sem("y_ready")

        def tasks(g):
            return g + 3

        def task_target(i, mix, val):
            if i < 2 or i >= 6:
                half = 1 if i < 2 else 0
                return mix[:, i % 2, half * BANK:(half + 1) * BANK]
            return val[:, 2 * (i - 2):2 * (i - 2) + 2]

        def turned(pT, blk):
            return pT[:, blk // QB, :, (blk % QB) * P:(blk % QB + 1) * P]

        def held(eng, count):
            if not isinstance(count, int):
                eng.compute_val(count)
            return count

        def over_images(eng, image, tail):
            for b in range(2):
                image(b, b, b * STEPS, 0)
            with eng.Fori(1, B // 2 - 1) as pair:
                first = eng.snap(pair * (2 * STEPS))
                for odd in range(2):
                    image(pair * 2 + odd, odd, first + odd * STEPS, pair)
            for b in range(B - 2, B):
                image(b, b % 2, b * STEPS, b // 2)
            tail(B, 0, B * STEPS, B // 2)

        block = ctx.enter_context(nc.Block())

        @block.sync
        def _(sp):
            def load_x(b, odd):
                sp.dma_start(x_sb[:, odd], x_v[b]).then_inc(x_loaded[odd], DMA_INC)

            load_x(0, 0)
            sp.dma_start(qkv_rows[:], qkv_w.rearrange("(t p) c -> p t c", p=P)).then_inc(qkv_loaded, DMA_INC)
            sp.dma_start(proj_rows[:], proj_w.rearrange("(t p) c -> p t c", p=P)).then_inc(proj_loaded, DMA_INC)
            for tile, vector in ((gain_w, norm_w), (gain_b, norm_b), (out_b, proj_b)):
                sp.dma_start(tile[:], vector.rearrange("(t p) -> p t", p=P),
                             allow_slow_non_contiguous=True).then_inc(vectors_loaded, DMA_INC)
            load_x(1, 1)

            def load_again(b, half):
                if positive(b):
                    sp.wait_ge(stored[half], DMA_INC * b)
                sp.dma_start(y[:, half], x_half[b, half]).then_inc(again_loaded[half], DMA_INC)

            def store(b, half):
                sp.wait_ge(y_ready, CT * (HALVES * b + half + 1))
                sp.dma_start(out_half[b, half], y[:, half]).then_inc(stored[half], DMA_INC)

            def image(b, odd, g, pair):
                if within(b + 2, B):
                    sp.wait_ge(h_ready, CT * (b + 1))
                    load_x(b + 2, odd)
                for half in range(HALVES):
                    if positive(b):
                        store(b - 1, half)
                    load_again(b, half)

            def tail(b, odd, g, pair):
                for half in range(HALVES):
                    store(b - 1, half)

            over_images(sp, image, tail)
            for half in range(HALVES):
                sp.wait_ge(stored[half], DMA_INC * B)

        @block.gpsimd
        def _(pool):
            nc.gpsimd.memset(ident[:], 0.0).then_inc(zeroed, 1)
            pool.wait_ge(zeroed, 1)
            nc.gpsimd.affine_select(out=ident[:], in_=ident[:], compare_op=ALU.not_equal, fill=1.0, base=0,
                                    pattern=[[-1, P]], channel_multiplier=1).then_inc(ident_ready, 1)

            def normalise(c, odd, steps):
                pool.wait_ge(vectors_loaded, 3 * DMA_INC)
                pool.wait_ge(var_ready, c + 1)
                nc.gpsimd.tensor_tensor(rstd[:], var_eps[:], minus_half[:], ALU.pow).then_inc(rstd_ready, 1)
                pool.wait_ge(rstd_ready, c + 1)
                nc.gpsimd.tensor_tensor(gain[:], rstd[:], gain_w[:], ALU.mult).then_inc(gain_ready, 1)
                pool.wait_ge(vectors_loaded, 3 * DMA_INC)
                pool.wait_ge(gain_ready, c + 1)
                for t in range(CT):
                    nc.gpsimd.tensor_scalar(x_sb[:, odd, t], x_sb[:, odd, t], mu[:, odd, t:t + 1],
                                            gain[:, t:t + 1], ALU.subtract, ALU.mult).then_inc(centred, 1)
                all_centred = held(pool, CT * (c + 1))
                scores_before = held(pool, steps - STEPS)
                pool.wait_ge(vectors_loaded, 3 * DMA_INC)
                if positive(scores_before):
                    pool.wait_ge(scores_done, scores_before)
                pool.wait_ge(centred, all_centred)
                for t in range(CT):
                    nc.gpsimd.tensor_scalar(h_hi[:, odd, t], x_sb[:, odd, t], gain_b[:, t:t + 1], None,
                                            ALU.add).then_inc(h_hi_ready, 1)
                pool.wait_ge(vectors_loaded, 3 * DMA_INC)
                pool.wait_ge(h_hi_ready, CT * (c + 1))
                for t in range(CT):
                    nc.gpsimd.tensor_scalar(x_sb[:, odd, t], x_sb[:, odd, t], gain_b[:, t:t + 1], None,
                                            ALU.add).then_inc(h_full, 1)
                for t in range(CT):
                    pool.wait_ge(h_full, CT * c + t + 1)
                    nc.gpsimd.tensor_tensor(h_lo[:, odd, t], x_sb[:, odd, t], h_hi[:, odd, t].bitcast(F32),
                                            ALU.subtract).then_inc(h_ready, 1)

            pool.wait_ge(half_ready, 1)
            normalise(0, 0, 0)

            def image(b, odd, g, pair):
                if within(b + 1, B):
                    normalise(b + 1, 1 - odd, g + STEPS)

            over_images(pool, image, lambda *_: None)

        @block.scalar
        def _(act):
            act.wait_ge(projT_done, 1)
            nc.scalar.copy(projT[:], ps_scores[:, 0:CT * C]).then_inc(projT_ready, 1)
            act.wait_ge(mixw_done, 1)
            nc.scalar.mul(mixw_hi[:], ps_turn[:, 0:4], SCALE).then_inc(fold_hi, 1)
            act.wait_ge(valw_done, 1)
            nc.scalar.copy(valw_hi[:], ps_turn[:, 4:8]).then_inc(fold_hi, 1)

            def task_high(b, i, g):
                act.wait_ge(task_done, tasks(g))
                nc.scalar.copy(task_target(i, mix_hi, val_hi), ps_task[:, i % 2]).then_inc(task_hi, 1)

            task_high(-1, 6, -2)
            task_high(-1, 7, -1)

            def step(b, i, g):
                if within(g - 1, LAST):
                    act.wait_ge(turn_done, g)
                    blk = (i - 1) % STEPS
                    nc.scalar.copy(turned(pT_hi, blk), ps_turn[:]).then_inc(pT_hi_ready, 1)
                if within(g, LAST):
                    act.wait_ge(max_ready, g + 1)
                    nc.scalar.activation(probs[:, i % 2], ps_scores[:], ACT.Exp, bias=neg_max[:, i % 2:i % 2 + 1],
                                         accum_out=row_sum[:, i % 2:i % 2 + 1]).then_inc(exp_done, 1)
                if within(g + 2, LAST):
                    task_high(b, i, g)

            def image(b, odd, g, pair):
                for i in range(STEPS):
                    step(b, i, g + i)

            over_images(act, image, lambda b, odd, g, pair: step(b, 0, g))

        @block.vector
        def _(dve):
            nc.vector.memset(minus_half[:], -0.5).then_inc(half_ready, 1)
            nc.vector.memset(group_mean[:], 0.0).then_inc(mean_zeroed, 1)
            dve.wait_ge(mean_zeroed, 1)
            for k in range(P // GROUP):
                members = slice(k * GROUP, (k + 1) * GROUP)
                nc.vector.memset(group_mean[members, members], 1.0 / GROUP).then_inc(const_ready, 1)

            dve.wait_ge(fold_hi, 1)
            nc.vector.scalar_tensor_tensor(mixw_lo[:], ps_turn[:, 0:4], SCALE, mixw_hi[:].bitcast(F32),
                                           ALU.mult, ALU.subtract).then_inc(fold_lo, 1)
            dve.wait_ge(fold_hi, 2)
            nc.vector.tensor_tensor(valw_lo[:], ps_turn[:, 4:8], valw_hi[:].bitcast(F32),
                                    ALU.subtract).then_inc(fold_lo, 1)

            def channel_stats(c, odd, pair, t):
                if t == 0:
                    dve.wait_ge(x_loaded[odd], DMA_INC * (pair + 1))
                for k in range(HALVES):
                    nc.vector.bn_stats(bn[:, t, k], x_sb[:, odd, t, k * BANK:(k + 1) * BANK]).then_inc(bn_ready, 1)
                before = held(dve, c)
                all_stats = held(dve, HALVES * (CT * c + t + 1))
                dve.wait_ge(x_loaded[0], DMA_INC)
                if t == 0 and positive(c):
                    dve.wait_ge(spread_ready, before)
                dve.wait_ge(bn_ready, all_stats)
                nc.vector.bn_aggr(chan[:, t], bn[:, t]).then_inc(chan_ready, 1)

            def group_stats(c, odd, ps_mean):
                dve.wait_ge(mean_done, c + 1)
                nc.vector.tensor_tensor(dev[:], chan[:, :, 0], ps_mean, ALU.subtract).then_inc(dev_ready, 1)
                if positive(c - 1):
                    dve.wait_ge(centred, CT * (c - 1))
                nc.vector.tensor_copy(mu[:, odd], ps_mean).then_inc(dev_ready, 1)
                dve.wait_ge(dev_ready, 2 * (c + 1))
                nc.vector.tensor_tensor(dev2[:], dev[:], dev[:], ALU.mult).then_inc(dev2_ready, 1)
                dve.wait_ge(dev2_ready, c + 1)
                nc.vector.tensor_tensor(spread[:], dev2[:], chan[:, :, 1], ALU.add).then_inc(spread_ready, 1)

            def group_var(c, ps_var):
                dve.wait_ge(var_done, c + 1)
                if positive(c):
                    dve.wait_ge(rstd_ready, c)
                nc.vector.tensor_scalar(var_eps[:], ps_var, EPS, None, ALU.add).then_inc(var_ready, 1)

            def task_low(b, i, g):
                dve.wait_ge(task_hi, tasks(g))
                nc.vector.tensor_tensor(task_target(i, mix_lo, val_lo), ps_task[:, i % 2],
                                        task_target(i, mix_hi, val_hi).bitcast(F32), ALU.subtract).then_inc(task_lo, 1)

            for t in range(CT):
                channel_stats(0, 0, 0, t)
            group_stats(0, 0, ps_out[:, 0, 0:CT])
            group_var(0, ps_out[:, 1, 0:CT])
            for t in range(CT):
                channel_stats(1, 1, 0, t)
            task_low(-1, 6, -2)
            task_low(-1, 7, -1)
            group_stats(1, 1, ps_task[:, 0, 0:CT])

            def residual(b, half):
                dve.wait_ge(pv_done, HALVES * b + half + 1)
                dve.wait_ge(again_loaded[half], DMA_INC * (b + 1))
                for t in range(CT):
                    nc.vector.scalar_tensor_tensor(y[:, half, t], ps_out[:, t], out_b[:, t:t + 1], y[:, half, t],
                                                   ALU.add, ALU.add).then_inc(y_ready, 1)

            def step(b, i, g, odd, pair):
                s = i % 2
                if within(g, LAST):
                    dve.wait_ge(scores_done, g + 1)
                    nc.vector.tensor_reduce(neg_max[:, s:s + 1], ps_scores[:], AX_X, ALU.max,
                                            negate=True).then_inc(max_ready, 1)
                if within(g - 1, LAST):
                    blk = (i - 1) % STEPS
                    dve.wait_ge(pT_hi_ready, g)
                    nc.vector.tensor_tensor(turned(pT_lo, blk), ps_turn[:], turned(pT_hi, blk).bitcast(F32),
                                            ALU.subtract).then_inc(pT_lo_ready, 1)
                if within(g, LAST):
                    dve.wait_ge(exp_done, g + 1)
                    nc.vector.reciprocal(row_inv[:, s:s + 1], row_sum[:, s:s + 1]).then_inc(inv_ready, 1)
                    dve.wait_ge(inv_ready, g + 1)
                    nc.vector.tensor_scalar(probs[:, s], probs[:, s], row_inv[:, s:s + 1], None,
                                            ALU.mult).then_inc(probs_ready, 1)
                if within(g + 2, LAST):
                    task_low(b, i, g)
                if i == 0 and within(b + 1, B):
                    group_var(b + 1, ps_task[:, 1, 0:CT])
                if i in (0, 4) and positive(b):
                    residual(b - 1, i // 4)
                if i in (5, 6) and within(b + 2, B):
                    channel_stats(b + 2, odd, pair + 1, i - 5)
                if i == 7 and within(b + 2, B):
                    group_stats(b + 2, odd, ps_task[:, 0, 0:CT])

            def image(b, odd, g, pair):
                for i in range(STEPS):
                    step(b, i, g + i, odd, pair)

            def tail(b, odd, g, pair):
                for i in range(PV_LAG):
                    step(b, i, g + i, odd, pair)

            over_images(dve, image, tail)

        @block.tensor
        def _(pe):
            def split_product(dst, weights, moving, start, stop):
                (w_hi, w_lo), (m_hi, m_lo) = weights, moving
                nc.tensor.matmul(dst, w_hi, m_hi, start=start, stop=False)
                nc.tensor.matmul(dst, w_hi, m_lo, start=False, stop=False)
                return nc.tensor.matmul(dst, w_lo, m_hi, start=False, stop=stop)

            pe.wait_ge(ident_ready, 1)
            pe.wait_ge(proj_loaded, DMA_INC)
            for k in range(CT):
                for t in range(CT):
                    at = k * C + t * P
                    last = nc.tensor.transpose(ps_scores[:, at:at + P], proj_rows[:, t, k * P:(k + 1) * P], ident[:])
            last.then_inc(projT_done, 1)
            pe.wait_ge(qkv_loaded, DMA_INC)
            for c in range(CT):
                for t in range(CT):
                    last = nc.tensor.matmul(ps_turn[:, 2 * c:2 * c + 2], qkv_rows[:, t, c * P:(c + 1) * P],
                                            qkv_rows[:, CT + t], start=(t == 0), stop=(t == CT - 1))
            last.then_inc(mixw_done, 1)
            pe.wait_ge(projT_ready, 1)
            for c in range(CT):
                for t in range(CT):
                    last = nc.tensor.matmul(ps_turn[:, 4 + 2 * c:6 + 2 * c], qkv_rows[:, 2 * CT + t, c * P:(c + 1) * P],
                                            projT[:, t], start=(t == 0), stop=(t == CT - 1))
            last.then_inc(valw_done, 1)

            def mean_over_groups(c, dst):
                pe.wait_ge(chan_ready, CT * (c + 1))
                nc.tensor.matmul(dst, group_mean[:], chan[:, :, 0], start=True, stop=True).then_inc(mean_done, 1)

            def var_over_groups(c, dst):
                pe.wait_ge(spread_ready, c + 1)
                nc.tensor.matmul(dst, group_mean[:], spread[:], start=True, stop=True).then_inc(var_done, 1)

            def task(b, i, g, odd):
                bank = ps_task[:, i % 2]
                if i < 2 or i >= 6:
                    half = 1 if i < 2 else 0
                    cols = slice(half * BANK, (half + 1) * BANK)
                    for k in range(CT):
                        chans = slice((i % 2) * P, (i % 2 + 1) * P)
                        last = split_product(bank, (mixw_hi[:, k, chans], mixw_lo[:, k, chans]),
                                             (h_hi[:, odd, k, cols], h_lo[:, odd, k, cols]), k == 0, k == CT - 1)
                else:
                    for m in range(2):
                        keys = slice((2 * (i - 2) + m) * P, (2 * (i - 2) + m + 1) * P)
                        for k in range(CT):
                            last = split_product(bank[:, m * C:(m + 1) * C],
                                                 (h_hi[:, odd, k, keys], h_lo[:, odd, k, keys]),
                                                 (valw_hi[:, k], valw_lo[:, k]), k == 0, k == CT - 1)
                last.then_inc(task_done, 1)

            pe.wait_ge(const_ready, P // GROUP)
            mean_over_groups(0, ps_out[:, 0, 0:CT])
            var_over_groups(0, ps_out[:, 1, 0:CT])
            pe.wait_ge(fold_lo, 2)
            pe.wait_ge(h_ready, CT)
            task(-1, 6, -2, 0)
            task(-1, 7, -1, 0)
            pe.wait_ge(task_lo, 1)
            mean_over_groups(1, ps_task[:, 0, 0:CT])

            def step(b, i, g, odd):
                if within(g, LAST):
                    if i == 0:
                        pe.wait_ge(task_lo, tasks(g - 1))
                    if i == 4:
                        pe.wait_ge(task_lo, tasks(g - 3))
                    if positive(g):
                        pe.wait_ge(exp_done, g)
                    q = slice(i * P, (i + 1) * P)
                    for half in range(HALVES):
                        cols = slice(half * BANK, (half + 1) * BANK)
                        for k in range(CT):
                            last = split_product(ps_scores[:, cols], (mix_hi[:, k, q], mix_lo[:, k, q]),
                                                 (h_hi[:, odd, k, cols], h_lo[:, odd, k, cols]), k == 0, k == CT - 1)
                    last.then_inc(scores_done, 1)
                if within(g - 1, LAST):
                    pe.wait_ge(probs_ready, g)
                    if positive(g - 1):
                        pe.wait_ge(pT_lo_ready, g - 1)
                    for m in range(KB):
                        last = nc.tensor.transpose(ps_turn[:, m], probs[:, (i - 1) % 2, m * P:(m + 1) * P], ident[:])
                    last.then_inc(turn_done, 1)
                if i == 0 and within(b + 1, B):
                    pe.wait_ge(task_lo, tasks(g - 1))
                    var_over_groups(b + 1, ps_task[:, 1, 0:CT])
                if i == 7 and within(b + 2, B):
                    pe.wait_ge(task_lo, tasks(g - 1))
                    mean_over_groups(b + 2, ps_task[:, 0, 0:CT])
                if within(g + 2, LAST):
                    pe.wait_ge(task_lo, tasks(g - 2))
                    if i == 0 and within(b + 1, B):
                        pe.wait_ge(dev_ready, 2 * (b + 2))
                    if i == 1 and within(b + 1, B):
                        pe.wait_ge(var_ready, b + 2)
                    if i == 6:
                        pe.wait_ge(h_ready, CT * (b + 2))
                    task(b, i, g, 1 - odd if i >= 6 else odd)
                products(b, i, g)

            def products(b, i, g):
                if not within(g - PV_LAG, LAST):
                    return
                quarter = (i - PV_LAG) % QB
                half = 1 if PV_LAG - QB <= i < PV_LAG else 0
                if quarter == 0:
                    pe.wait_ge(pT_lo_ready, g - 1)
                    done = CT * (HALVES * b + (half if half == 0 else -1))
                    if positive(done):
                        pe.wait_ge(y_ready, done)
                if half == 0:
                    pe.wait_ge(task_lo, tasks(g - 3))
                for m in range(2 * quarter, 2 * quarter + 2):
                    for t in range(CT):
                        chans = slice(t * P, (t + 1) * P)
                        last = split_product(ps_out[:, t], (val_hi[:, m, chans], val_lo[:, m, chans]),
                                             (pT_hi[:, half, m], pT_lo[:, half, m]), m == 0, m == KB - 1)
                if quarter == QB - 1:
                    last.then_inc(pv_done, 1)

            def image(b, odd, g, pair):
                for i in range(STEPS):
                    step(b, i, g + i, odd)

            def tail(b, odd, g, pair):
                for i in range(PV_LAG):
                    step(b, i, g + i, odd)

            over_images(pe, image, tail)


_INS = ["x", "L0_conv_norm_w", "L0_conv_norm_b", "L0_conv_qkv_w", "L0_conv_proj_w", "L0_conv_proj_b"]


def kernel(**inputs):
    import numpy as _np
    import concourse.bacc as _bacc
    from concourse import mybir as _mybir
    from concourse.bass_utils import run_bass_kernel_spmd as _run

    nc = _bacc.Bacc("TRN2", target_bir_lowering=False, num_devices=1)
    arrays, args = {}, []
    shape = inputs["x"].shape
    for name in _INS:
        a = _np.ascontiguousarray(inputs[name])
        if name == "x":
            a = a.reshape(shape[0], shape[1], shape[2] * shape[3])
        arrays[f"in_{name}_dram"] = a
        args.append(nc.dram_tensor(f"in_{name}_dram", a.shape, _mybir.dt.from_np(a.dtype), kind="ExternalInput").ap())
    flat = (shape[0], shape[1], shape[2] * shape[3])
    args.append(nc.dram_tensor("out_dram", flat, _mybir.dt.float32, kind="ExternalOutput").ap())
    attention_block(nc, *args)
    r = _run(nc, [arrays], core_ids=[0])
    return r.results[0]["out_dram"].reshape(shape)
```

```python
from contextlib import ExitStack

import concourse.bass as bass
from concourse import mybir

ALU = mybir.AluOpType
ACT = mybir.ActivationFunctionType
AX_X = mybir.AxisListType.X
F32 = mybir.dt.float32
F32R = mybir.dt.float32r

P = 128
GROUPS = 8
EPS = 1e-5
DMA_INC = 16
BANK = 512
STEPS = 8


def positive(count):
    return not isinstance(count, int) or count > 0


def within(value, end):
    return not isinstance(value, int) or 0 <= value < end


def attention_block(nc, x, norm_w, norm_b, qkv_w, proj_w, proj_b, out):
    B, C, N = x.shape
    CT = C // P
    KB = N // P
    Q = 32
    QUARTERS = P // Q
    HALVES = N // BANK
    QB = BANK // P
    SCALE = float(C) ** -0.5
    GROUP = C // GROUPS
    OT = 3 * C // P
    LAST = B * STEPS
    assert KB == STEPS and HALVES == 2 and CT == 2 and P % GROUP == 0 and B % 2 == 0

    x_v = x.rearrange("b (t p) n -> b p t n", p=P)
    x_half = x.rearrange("b (t p) (h n) -> b h p t n", p=P, h=HALVES)
    out_half = out.rearrange("b (t p) (h n) -> b h p t n", p=P, h=HALVES)

    with ExitStack() as ctx:
        def sb(name, shape, dt=F32):
            return ctx.enter_context(nc.sbuf_tensor(name, shape, dt))

        def ps(name, shape):
            return ctx.enter_context(nc.psum_tensor(name, shape, F32))

        def sem(name):
            return ctx.enter_context(nc.semaphore(name))

        flipped = sb("flipped", [P, 2, 2, N])
        moved = sb("moved", [P, 2, 2, QUARTERS, N // QUARTERS])
        qkv_rows = flipped[:].rearrange("p a b n -> p (a b n)")[:, 0:OT * C].rearrange("p (t c) -> p t c", c=C)
        first_rows = moved[:].rearrange("p a b s n -> p (a b s n)")[:, 0:2 * CT * C].rearrange("p (t c) -> p t c", c=C)
        proj_rows = first_rows[:, 0:CT]
        projT = first_rows[:, CT:2 * CT]
        mixw_hi = sb("mixw_hi", [P, CT, C], F32R)
        mixw_lo = sb("mixw_lo", [P, CT, C], F32R)
        valw_hi = sb("valw_hi", [P, CT, C], F32R)
        valw_lo = sb("valw_lo", [P, CT, C], F32R)
        gain_w = sb("gain_w", [P, CT])
        gain_b = sb("gain_b", [P, CT])
        out_b = sb("out_b", [P, CT])
        ident = sb("ident", [P, P])
        group_mean = sb("group_mean", [P, P])
        minus_half = sb("minus_half", [P, CT])

        x_sb = sb("x_sb", [P, 2, CT, N])
        bn = sb("bn", [P, CT, HALVES, 6])
        chan = sb("chan", [P, CT, 2])
        mu = sb("mu", [P, 2, CT])
        dev = sb("dev", [P, CT])
        dev2 = sb("dev2", [P, CT])
        spread = sb("spread", [P, CT])
        var_eps = sb("var_eps", [P, CT])
        rstd = sb("rstd", [P, CT])
        gain = sb("gain", [P, CT])
        h_hi = sb("h_hi", [P, 2, CT, N], F32R)
        h_lo = sb("h_lo", [P, 2, CT, N], F32R)

        mix_hi = sb("mix_hi", [P, CT, N], F32R)
        mix_lo = sb("mix_lo", [P, CT, N], F32R)
        val_hi = sb("val_hi", [P, KB, C], F32R)
        val_lo = sb("val_lo", [P, KB, C], F32R)
        neg_max = sb("neg_max", [P, 2])
        row_sum = sb("row_sum", [P, 2])
        row_inv = sb("row_inv", [P, 2])
        probs = sb("probs", [P, 2, N])
        pT_hi = sb("pT_hi", [P, HALVES, KB, BANK], F32R)
        pT_lo = sb("pT_lo", [P, HALVES, KB, BANK], F32R)
        y = sb("y", [P, HALVES, CT, BANK])

        ps_scores = ps("ps_scores", [P, 2, N])
        ps_fold = ps_scores[:, 1].rearrange("p (w t c) -> p w t c", w=2, t=CT)
        ps_task = ps("ps_task", [P, 2, BANK])
        ps_out = ps("ps_out", [P, CT, BANK])

        first_loaded = sem("first_loaded")
        qk_loaded = sem("qk_loaded")
        v_loaded = sem("v_loaded")
        proj_loaded = sem("proj_loaded")
        vectors_loaded = sem("vectors_loaded")
        x_loaded = [sem("x_loaded_even"), sem("x_loaded_odd")]
        again_loaded = [sem("again_loaded_0"), sem("again_loaded_1")]
        stored = [sem("stored_0"), sem("stored_1")]
        zeroed = sem("zeroed")
        ident_ready = sem("ident_ready")
        half_ready = sem("half_ready")
        mean_zeroed = sem("mean_zeroed")
        const_ready = sem("const_ready")
        projT_done = sem("projT_done")
        projT_ready = sem("projT_ready")
        mixw_done = sem("mixw_done")
        valw_done = sem("valw_done")
        fold_hi = sem("fold_hi")
        fold_lo = sem("fold_lo")
        bn_ready = sem("bn_ready")
        chan_ready = sem("chan_ready")
        mean_done = sem("mean_done")
        dev_ready = sem("dev_ready")
        dev2_ready = sem("dev2_ready")
        spread_ready = sem("spread_ready")
        var_done = sem("var_done")
        var_ready = sem("var_ready")
        rstd_ready = sem("rstd_ready")
        gain_ready = sem("gain_ready")
        centred = sem("centred")
        h_hi_ready = sem("h_hi_ready")
        h_ready = sem("h_ready")
        first_centred = sem("first_centred")
        first_hi_ready = sem("first_hi_ready")
        first_ready = sem("first_ready")
        turned_done = sem("turned_done")
        last_tile_done = sem("last_tile_done")
        task_done = sem("task_done")
        task_hi = sem("task_hi")
        task_lo = sem("task_lo")
        scores_done = sem("scores_done")
        max_ready = sem("max_ready")
        exp_done = sem("exp_done")
        inv_ready = sem("inv_ready")
        scaled = sem("scaled")
        flip_ready = sem("flip_ready")
        pair_moved = [sem(f"pair_moved_{k}") for k in range(STEPS // 2)]
        pT_hi_ready = sem("pT_hi_ready")
        pT_lo_ready = sem("pT_lo_ready")
        pv_done = sem("pv_done")
        y_ready = sem("y_ready")

        TASKS = [("last", 2), ("last", 3), ("mix", (0, 1)), ("mix", (1, 1)), ("next", (0, 0)), ("values", 0),
                 ("next", (1, 0)), ("values", 1)]

        def tasks_of(b, i):
            exists = {"last": positive(b) and within(b - 1, B), "mix": within(b, B), "values": within(b, B),
                      "next": within(b + 1, B)}
            kind, arg = TASKS[i]
            return [(kind, arg)] if exists[kind] else []

        def left_out(b, k):
            following = [n for n, (kind, _) in enumerate(TASKS) if kind == "next"]
            if not isinstance(b, int) or b < B - 1:
                return 0
            return len([n for n in following if b == B or n < k])

        def task_count(b, first, k):
            return first + k + 1 - left_out(b, k)

        def bank_of(b, k):
            return (k - left_out(b, k)) % 2

        def task_target(kind, arg, mix, val):
            if kind in ("mix", "next"):
                tile, half = arg
                return mix[:, tile, half * BANK:(half + 1) * BANK]
            return val[:, 2 * arg:2 * arg + 2]

        def turned(pT, i):
            blk = i % STEPS
            return pT[:, blk // QB, :, (blk % QB) * P:(blk % QB + 1) * P].rearrange("p j (s r) -> p j s r", r=Q)

        def arrived(i):
            blk = i % STEPS
            return moved[:, blk // 2 % 2, blk % 2].rearrange("p s (j r) -> p j s r", r=Q)

        def held(eng, count):
            if not isinstance(count, int):
                eng.compute_val(count)
            return count

        def over_steps(eng, step):
            def image(b, odd, g, pair):
                for i in range(STEPS):
                    step(b, i, g + i, odd, pair)

            for b in range(2):
                image(b, b, b * STEPS, 0)
            with eng.Fori(1, B // 2 - 1) as pair:
                first = eng.snap(pair * (2 * STEPS))
                for odd in range(2):
                    image(pair * 2 + odd, odd, first + odd * STEPS, pair)
            for b in range(B - 2, B):
                image(b, b % 2, b * STEPS, b // 2)
            for i in range(STEPS + 1):
                step(B + i // STEPS, i % STEPS, B * STEPS + i, i // STEPS, (B + i // STEPS) // 2)

        block = ctx.enter_context(nc.Block())

        @block.sync
        def _(sp):
            def load_x(b, odd):
                sp.dma_start(x_sb[:, odd], x_v[b]).then_inc(x_loaded[odd], DMA_INC)

            for t in range(CT):
                sp.dma_start(x_sb[:, 0, t], x_v[0, :, t]).then_inc(x_loaded[0] if t else first_loaded, DMA_INC)
            qkv_v = qkv_w.rearrange("(t p) c -> p t c", p=P)
            sp.dma_start(qkv_rows[:, 0:2 * CT], qkv_v[:, 0:2 * CT]).then_inc(qk_loaded, DMA_INC)
            for tile, vector in ((gain_w, norm_w), (gain_b, norm_b), (out_b, proj_b)):
                sp.dma_start(tile[:], vector.rearrange("(t p) -> p t", p=P),
                             allow_slow_non_contiguous=True).then_inc(vectors_loaded, DMA_INC)
            sp.dma_start(proj_rows[:], proj_w.rearrange("(t p) c -> p t c", p=P)).then_inc(proj_loaded, DMA_INC)
            sp.dma_start(qkv_rows[:, 2 * CT:], qkv_v[:, 2 * CT:]).then_inc(v_loaded, DMA_INC)
            load_x(1, 1)

            def load_again(b, half):
                if positive(b):
                    sp.wait_ge(stored[half], DMA_INC * b)
                sp.dma_start(y[:, half], x_half[b, half]).then_inc(again_loaded[half], DMA_INC)

            def store(b, half):
                held(sp, b * (C * N) * 4)
                sp.wait_ge(y_ready, CT * (HALVES * b + half + 1))
                sp.dma_start(out_half[b, half], y[:, half]).then_inc(stored[half], DMA_INC)

            def step(b, i, g, odd, pair):
                if i == 0 and within(b + 2, B):
                    sp.wait_ge(h_ready, CT * (b + 1))
                    load_x(b + 2, odd)
                if i % 2 == 1 and within(g, LAST - 2):
                    flips, splits = held(sp, g + 1), held(sp, g - 3)
                    sp.wait_ge(flip_ready, flips)
                    if positive(splits):
                        sp.wait_ge(pT_lo_ready, splits)
                    at = i // 2 % 2
                    for s in range(QUARTERS):
                        for d in range(QUARTERS):
                            sp.dma_start(moved[d * Q:(d + 1) * Q, at, :, s],
                                         flipped[s * Q:(s + 1) * Q, at, :, d * (N // QUARTERS):(d + 1) * (N // QUARTERS)]
                                         ).then_inc(pair_moved[i // 2], DMA_INC)
                if i == 2 and positive(b - 1):
                    store(b - 2, 1)
                if i == 2 and positive(b) and within(b - 1, B):
                    load_again(b - 1, 1)
                if i == 6 and positive(b):
                    store(b - 1, 0)
                if i == 6 and within(b, B):
                    load_again(b, 0)

            over_steps(sp, step)
            for t in range(CT):
                sp.wait_ge(y_ready, CT * (HALVES * B - 1) + t + 1)
                sp.dma_start(out_half[B - 1, 1, :, t], y[:, 1, t]).then_inc(stored[1], DMA_INC)
            sp.wait_ge(stored[0], DMA_INC * B)
            sp.wait_ge(stored[1], DMA_INC * (B - 1 + CT))

        @block.gpsimd
        def _(pool):
            nc.gpsimd.memset(ident[:], 0.0).then_inc(zeroed, 1)
            pool.wait_ge(zeroed, 1)
            nc.gpsimd.affine_select(out=ident[:], in_=ident[:], compare_op=ALU.not_equal, fill=1.0, base=0,
                                    pattern=[[-1, P]], channel_multiplier=1).then_inc(ident_ready, 1)

            def deviation(c):
                pool.wait_ge(var_ready, c + 1)
                if positive(c):
                    pool.wait_ge(gain_ready, c)
                nc.gpsimd.tensor_tensor(rstd[:], var_eps[:], minus_half[:], ALU.pow).then_inc(rstd_ready, 1)

            pool.wait_ge(half_ready, 1)
            deviation(0)

            def step(b, i, g, odd, pair):
                if i == 1 and within(b + 1, B):
                    deviation(b + 1)

            over_steps(pool, step)

        @block.scalar
        def _(act):
            act.wait_ge(mixw_done, 1)
            nc.scalar.mul(mixw_hi[:], ps_fold[:, 0], SCALE).then_inc(fold_hi, 1)
            act.wait_ge(projT_done, 1)
            nc.scalar.copy(projT, ps_scores[:, 0, 0:CT * C]).then_inc(projT_ready, 1)

            def task_high(b, first, k, kind, arg):
                act.wait_ge(task_done, task_count(b, first, k))
                nc.scalar.copy(task_target(kind, arg, mix_hi, val_hi), ps_task[:, bank_of(b, k)]).then_inc(task_hi, 1)

            def norm_high(c, odd, t):
                act.wait_ge(vectors_loaded, 3 * DMA_INC)
                act.wait_ge(centred, CT * c + t + 1)
                nc.scalar.activation(h_hi[:, odd, t], x_sb[:, odd, t], ACT.Identity,
                                     bias=gain_b[:, t:t + 1]).then_inc(h_hi_ready, 1)

            act.wait_ge(vectors_loaded, 3 * DMA_INC)
            for half in range(HALVES):
                cols = slice(half * BANK, (half + 1) * BANK)
                for t in range(CT):
                    act.wait_ge(centred if half else first_centred, t + 1)
                    nc.scalar.activation(h_hi[:, 0, t, cols], x_sb[:, 0, t, cols], ACT.Identity,
                                         bias=gain_b[:, t:t + 1]).then_inc(h_hi_ready if half else first_hi_ready, 1)
            act.wait_ge(valw_done, 1)
            nc.scalar.copy(valw_hi[:], ps_fold[:, 1]).then_inc(fold_hi, 1)
            for tile in range(CT):
                task_high(0, 0, tile, "next", (tile, 0))

            def step(b, i, g, odd, pair):
                s = i % 2
                if within(g - 4, LAST):
                    pairs = (g - 4 - (i - 4) % STEPS) * (QUARTERS * QUARTERS * DMA_INC // STEPS)
                    if i % QB == 0 and positive(HALVES * b + i // QB - 2):
                        act.wait_ge(pv_done, HALVES * b + i // QB - 2)
                    if within(g - 4, LAST - 2):
                        act.wait_ge(pair_moved[(i - 4) % STEPS // 2], pairs + QUARTERS * QUARTERS * DMA_INC)
                        nc.scalar.copy(turned(pT_hi, i - 4), arrived(i - 4)).then_inc(pT_hi_ready, 1)
                    else:
                        act.wait_ge(turned_done, g - 3 - (LAST - 2))
                        nc.scalar.copy(pT_hi[:, 1, :, (i - 4) % QB * P:((i - 4) % QB + 1) * P],
                                       ps_scores[:, s].rearrange("p (j q) -> p j q", q=P)).then_inc(pT_hi_ready, 1)
                if within(g, LAST):
                    act.wait_ge(max_ready, g + 1)
                    if within(g, LAST - 2):
                        exps, scores = probs[:, s], ps_scores[:, s]
                    else:
                        exps = probs[:, s].rearrange("p (j d a) -> p d j a", d=QUARTERS, a=Q)
                        scores = ps_scores[:, s].rearrange("p (d j a) -> p d j a", d=QUARTERS, a=Q)
                    nc.scalar.activation(exps, scores, ACT.Exp, bias=neg_max[:, s:s + 1],
                                         accum_out=row_sum[:, s:s + 1]).then_inc(exp_done, 1)
                for kind, arg in tasks_of(b, i):
                    task_high(b, g - i, i, kind, arg)
                if within(g, LAST):
                    act.wait_ge(inv_ready, g + 1)
                    nc.scalar.mul(probs[:, s], probs[:, s], row_inv[:, s:s + 1]).then_inc(scaled, 1)
                if i in (1, 2) and within(b + 1, B):
                    norm_high(b + 1, 1 - odd, i - 1)

            over_steps(act, step)

        @block.vector
        def _(dve):
            nc.vector.memset(minus_half[:], -0.5).then_inc(half_ready, 1)
            nc.vector.memset(group_mean[:], 0.0).then_inc(mean_zeroed, 1)
            dve.wait_ge(mean_zeroed, 1)
            for k in range(P // GROUP):
                members = slice(k * GROUP, (k + 1) * GROUP)
                nc.vector.memset(group_mean[members, members], 1.0 / GROUP).then_inc(const_ready, 1)

            def channel_stats(c, odd, pair, t):
                if not positive(c):
                    dve.wait_ge(x_loaded[0] if t else first_loaded, DMA_INC)
                elif t == 0:
                    dve.wait_ge(x_loaded[odd], DMA_INC * (pair + 1))
                for k in range(HALVES):
                    nc.vector.bn_stats(bn[:, t, k], x_sb[:, odd, t, k * BANK:(k + 1) * BANK]).then_inc(bn_ready, 1)
                before = held(dve, c)
                all_stats = held(dve, HALVES * (CT * c + t + 1))
                dve.wait_ge(x_loaded[0], DMA_INC)
                if t == 0 and positive(c):
                    dve.wait_ge(spread_ready, before)
                dve.wait_ge(bn_ready, all_stats)
                nc.vector.bn_aggr(chan[:, t], bn[:, t]).then_inc(chan_ready, 1)

            def group_stats(c, odd, ps_mean):
                dve.wait_ge(mean_done, c + 1)
                nc.vector.tensor_tensor(dev[:], chan[:, :, 0], ps_mean, ALU.subtract).then_inc(dev_ready, 1)
                nc.vector.tensor_copy(mu[:, odd], ps_mean).then_inc(dev_ready, 1)
                dve.wait_ge(dev_ready, 2 * (c + 1))
                nc.vector.tensor_tensor(dev2[:], dev[:], dev[:], ALU.mult).then_inc(dev2_ready, 1)
                dve.wait_ge(dev2_ready, c + 1)
                nc.vector.tensor_tensor(spread[:], dev2[:], chan[:, :, 1], ALU.add).then_inc(spread_ready, 1)

            def group_var(c, ps_var):
                dve.wait_ge(var_done, c + 1)
                if positive(c):
                    dve.wait_ge(rstd_ready, c)
                nc.vector.tensor_scalar(var_eps[:], ps_var, EPS, None, ALU.add).then_inc(var_ready, 1)

            def centre(c, odd):
                dve.wait_ge(vectors_loaded, 3 * DMA_INC)
                dve.wait_ge(rstd_ready, c + 1)
                nc.vector.tensor_tensor(gain[:], rstd[:], gain_w[:], ALU.mult).then_inc(gain_ready, 1)
                dve.wait_ge(gain_ready, c + 1)
                first = isinstance(c, int) and c == 0
                for cols in [slice(0, BANK), slice(BANK, N)] if first else [slice(0, N)]:
                    for t in range(CT):
                        nc.vector.tensor_scalar(x_sb[:, odd, t, cols], x_sb[:, odd, t, cols], mu[:, odd, t:t + 1],
                                                gain[:, t:t + 1], ALU.subtract, ALU.mult
                                                ).then_inc(centred if cols.stop == N else first_centred, 1)

            def norm_low(c, odd, t):
                dve.wait_ge(h_hi_ready, CT * c + t + 1)
                nc.vector.scalar_tensor_tensor(h_lo[:, odd, t], x_sb[:, odd, t], gain_b[:, t:t + 1],
                                               h_hi[:, odd, t].bitcast(F32), ALU.add,
                                               ALU.subtract).then_inc(h_ready, 1)

            def task_low(b, first, k, kind, arg):
                dve.wait_ge(task_hi, task_count(b, first, k))
                nc.vector.tensor_tensor(task_target(kind, arg, mix_lo, val_lo), ps_task[:, bank_of(b, k)],
                                        task_target(kind, arg, mix_hi, val_hi).bitcast(F32),
                                        ALU.subtract).then_inc(task_lo, 1)

            for t in range(CT):
                channel_stats(0, 0, 0, t)
            group_stats(0, 0, ps_out[:, 0, 0:CT])
            group_var(0, ps_out[:, 1, 0:CT])
            centre(0, 0)
            dve.wait_ge(fold_hi, 1)
            nc.vector.scalar_tensor_tensor(mixw_lo[:], ps_fold[:, 0], SCALE, mixw_hi[:].bitcast(F32),
                                           ALU.mult, ALU.subtract).then_inc(fold_lo, 1)
            for half in range(HALVES):
                cols = slice(half * BANK, (half + 1) * BANK)
                for t in range(CT):
                    dve.wait_ge(h_hi_ready if half else first_hi_ready, t + 1)
                    nc.vector.scalar_tensor_tensor(h_lo[:, 0, t, cols], x_sb[:, 0, t, cols], gain_b[:, t:t + 1],
                                                   h_hi[:, 0, t, cols].bitcast(F32), ALU.add,
                                                   ALU.subtract).then_inc(h_ready if half else first_ready, 1)
            dve.wait_ge(fold_hi, 2)
            nc.vector.tensor_tensor(valw_lo[:], ps_fold[:, 1], valw_hi[:].bitcast(F32),
                                    ALU.subtract).then_inc(fold_lo, 1)
            for tile in range(CT):
                task_low(0, 0, tile, "next", (tile, 0))
            for t in range(CT):
                channel_stats(1, 1, 0, t)

            def residual(b, half):
                last = isinstance(b, int) and b == B - 1 and half == HALVES - 1
                if not last:
                    dve.wait_ge(pv_done, HALVES * b + half + 1)
                dve.wait_ge(again_loaded[half], DMA_INC * (b + 1))
                for t in range(CT):
                    if last:
                        dve.wait_ge(last_tile_done, t + 1)
                    nc.vector.scalar_tensor_tensor(y[:, half, t], ps_out[:, t], out_b[:, t:t + 1], y[:, half, t],
                                                   ALU.add, ALU.add).then_inc(y_ready, 1)

            def step(b, i, g, odd, pair):
                s = i % 2
                if within(g, LAST):
                    dve.wait_ge(scores_done, g + 1)
                    nc.vector.tensor_reduce(neg_max[:, s:s + 1], ps_scores[:, s], AX_X, ALU.max,
                                            negate=True).then_inc(max_ready, 1)
                if within(g - 4, LAST):
                    dve.wait_ge(pT_hi_ready, g - 3)
                    if within(g - 4, LAST - 2):
                        nc.vector.tensor_tensor(turned(pT_lo, i - 4), arrived(i - 4), turned(pT_hi, i - 4).bitcast(F32),
                                                ALU.subtract).then_inc(pT_lo_ready, 1)
                    else:
                        queries = slice((i - 4) % QB * P, ((i - 4) % QB + 1) * P)
                        nc.vector.tensor_tensor(pT_lo[:, 1, :, queries],
                                                ps_scores[:, s].rearrange("p (j q) -> p j q", q=P),
                                                pT_hi[:, 1, :, queries].bitcast(F32), ALU.subtract
                                                ).then_inc(pT_lo_ready, 1)
                if i == 0 and within(b + 1, B):
                    group_stats(b + 1, 1 - odd, ps_task[:, 1, 0:CT])
                if i == 1 and within(b + 1, B):
                    group_var(b + 1, ps_task[:, 0, 0:CT])
                if within(g, LAST):
                    dve.wait_ge(exp_done, g + 1)
                    nc.vector.reciprocal(row_inv[:, s:s + 1], row_sum[:, s:s + 1]).then_inc(inv_ready, 1)
                for kind, arg in tasks_of(b, i):
                    task_low(b, g - i, i, kind, arg)
                if i in (2, 3) and within(b + 1, B):
                    norm_low(b + 1, 1 - odd, i - 2)
                if i in (5, 6) and within(b + 2, B):
                    channel_stats(b + 2, odd, pair + 1, i - 5)
                if i == STEPS - 1 and positive(b):
                    residual(b - 1, 1)
                if i == QB - 1 and positive(b):
                    residual(b - 1, 0)
                if within(g, LAST - 2):
                    dve.wait_ge(scaled, g + 1)
                    nc.vector.transpose(flipped[:, i // 2 % 2, s], probs[:, s]).then_inc(flip_ready, 1)
                if i == 1 and within(b + 1, B):
                    centre(b + 1, 1 - odd)

            over_steps(dve, step)

        @block.tensor
        def _(pe):
            def split_product(dst, weights, moving, start, stop):
                (w_hi, w_lo), (m_hi, m_lo) = weights, moving
                nc.tensor.matmul(dst, w_hi, m_hi, start=start, stop=False)
                nc.tensor.matmul(dst, w_hi, m_lo, start=False, stop=False)
                return nc.tensor.matmul(dst, w_lo, m_hi, start=False, stop=stop)

            def mean_over_groups(c, dst):
                pe.wait_ge(chan_ready, CT * (c + 1))
                nc.tensor.matmul(dst, group_mean[:], chan[:, :, 0], start=True, stop=True).then_inc(mean_done, 1)

            def var_over_groups(c, dst):
                pe.wait_ge(spread_ready, c + 1)
                nc.tensor.matmul(dst, group_mean[:], spread[:], start=True, stop=True).then_inc(var_done, 1)

            def task(turn, kind, arg, odd):
                bank = ps_task[:, turn]
                if kind in ("mix", "next"):
                    tile, half = arg
                    chans = slice(tile * P, (tile + 1) * P)
                    cols = slice(half * BANK, (half + 1) * BANK)
                    for k in range(CT):
                        last = split_product(bank, (mixw_hi[:, k, chans], mixw_lo[:, k, chans]),
                                             (h_hi[:, odd, k, cols], h_lo[:, odd, k, cols]), k == 0, k == CT - 1)
                else:
                    for m in range(2):
                        keys = slice((2 * arg + m) * P, (2 * arg + m + 1) * P)
                        for k in range(CT):
                            last = split_product(bank[:, m * C:(m + 1) * C],
                                                 (h_hi[:, odd, k, keys], h_lo[:, odd, k, keys]),
                                                 (valw_hi[:, k], valw_lo[:, k]), k == 0, k == CT - 1)
                last.then_inc(task_done, 1)

            def keys_by_quarter(h, odd, k, half):
                return h[:, odd, k].rearrange("p (j d a) -> p d j a", d=QUARTERS, a=Q)[:, 2 * half:2 * half + 2]

            pe.wait_ge(const_ready, P // GROUP)
            mean_over_groups(0, ps_out[:, 0, 0:CT])
            pe.wait_ge(qk_loaded, DMA_INC)
            for c in range(CT):
                for t in range(CT):
                    last = nc.tensor.matmul(ps_fold[:, 0, c], qkv_rows[:, t, c * P:(c + 1) * P],
                                            qkv_rows[:, CT + t], start=(t == 0), stop=(t == CT - 1))
                if c == 0:
                    var_over_groups(0, ps_out[:, 1, 0:CT])
            last.then_inc(mixw_done, 1)
            pe.wait_ge(ident_ready, 1)
            pe.wait_ge(proj_loaded, DMA_INC)
            for k in range(CT):
                for t in range(CT):
                    at = k * C + t * P
                    last = nc.tensor.transpose(ps_scores[:, 0, at:at + P], proj_rows[:, t, k * P:(k + 1) * P], ident[:])
            last.then_inc(projT_done, 1)
            pe.wait_ge(v_loaded, DMA_INC)
            pe.wait_ge(projT_ready, 1)
            for c in range(CT):
                for t in range(CT):
                    last = nc.tensor.matmul(ps_fold[:, 1, c], qkv_rows[:, 2 * CT + t, c * P:(c + 1) * P],
                                            projT[:, t], start=(t == 0), stop=(t == CT - 1))
            last.then_inc(valw_done, 1)
            pe.wait_ge(fold_lo, 1)
            pe.wait_ge(first_ready, CT)
            for tile in range(CT):
                task(bank_of(0, tile), "next", (tile, 0), 0)

            def chunk_product(half, m, t):
                chans = slice(t * P, (t + 1) * P)
                return split_product(ps_out[:, t], (val_hi[:, m, chans], val_lo[:, m, chans]),
                                     (pT_hi[:, half, m], pT_lo[:, half, m]), m == 0, m == KB - 1)

            def products(b, i, g):
                half, quarter = i // QB, i % QB
                if quarter == 0:
                    pe.wait_ge(pT_lo_ready, g - 4)
                    if positive(HALVES * (b - 1) + half):
                        pe.wait_ge(y_ready, CT * (HALVES * (b - 1) + half))
                if half == 0:
                    if ("last", quarter) in TASKS:
                        pe.wait_ge(task_lo, task_count(b, g - i, TASKS.index(("last", quarter))))
                    else:
                        pe.wait_ge(task_lo, task_count(b - 1, g - i - STEPS, TASKS.index(("values", quarter))))
                for m in range(2 * quarter, 2 * quarter + 2):
                    for t in range(CT):
                        last = chunk_product(half, m, t)
                if quarter == QB - 1:
                    last.then_inc(pv_done, 1)

            def last_products():
                pe.wait_ge(pT_lo_ready, LAST)
                pe.wait_ge(y_ready, CT * (HALVES * B - 1))
                for t in range(CT):
                    for m in range(KB):
                        last = chunk_product(HALVES - 1, m, t)
                    last.then_inc(last_tile_done, 1)

            def step(b, i, g, odd, pair):
                s = i % 2
                if within(g, LAST):
                    if not positive(g):
                        pe.wait_ge(h_ready, CT)
                    if positive(g - 1):
                        pe.wait_ge(exp_done, g - 1)
                    q = slice(i * P, (i + 1) * P)
                    for k in range(CT):
                        if i == 0:
                            pe.wait_ge(task_lo, task_count(b - 1, g - STEPS, TASKS.index(("next", (k, 0))))
                                       if positive(b) else k + 1)
                        if i == QB:
                            pe.wait_ge(task_lo, task_count(b, g - i, TASKS.index(("mix", (k, 1)))))
                        for half in range(HALVES):
                            last = split_product(ps_scores[:, s, half * BANK:(half + 1) * BANK],
                                                 (mix_hi[:, k, q], mix_lo[:, k, q]),
                                                 (keys_by_quarter(h_hi, odd, k, half),
                                                  keys_by_quarter(h_lo, odd, k, half)), k == 0, k == CT - 1)
                    last.then_inc(scores_done, 1)
                for kind, arg in tasks_of(b, i):
                    pe.wait_ge(task_lo, task_count(b, g - i, i) - 2)
                    if i == 1 and within(b + 1, B):
                        pe.wait_ge(dev_ready, 2 * (b + 2))
                    if i == 2 and within(b + 1, B):
                        pe.wait_ge(var_ready, b + 2)
                    if kind == "next":
                        pe.wait_ge(h_ready, CT * (b + 2))
                    task(bank_of(b, i), kind, arg, odd if kind in ("mix", "values") else 1 - odd)
                if i == 0 and within(b + 1, B):
                    if positive(b):
                        pe.wait_ge(task_lo, task_count(b, g - i, -1))
                    mean_over_groups(b + 1, ps_task[:, 1, 0:CT])
                if i == 1 and within(b + 1, B):
                    pe.wait_ge(task_lo, task_count(b, g - i, 0))
                    var_over_groups(b + 1, ps_task[:, 0, 0:CT])
                if not within(g - 1, LAST - 2) and within(g - 1, LAST):
                    pe.wait_ge(scaled, g)
                    for j in range(KB):
                        keys = slice(j * P, (j + 1) * P)
                        last = nc.tensor.transpose(ps_scores[:, 1 - s, keys], probs[:, 1 - s, keys], ident[:])
                    last.then_inc(turned_done, 1)
                if within(g - STEPS, LAST - QB):
                    products(b, i, g)

            over_steps(pe, step)
            last_products()


_INS = ["x", "L0_conv_norm_w", "L0_conv_norm_b", "L0_conv_qkv_w", "L0_conv_proj_w", "L0_conv_proj_b"]


def kernel(**inputs):
    import numpy as _np
    import concourse.bacc as _bacc
    from concourse import mybir as _mybir
    from concourse.bass_utils import run_bass_kernel_spmd as _run

    nc = _bacc.Bacc("TRN2", target_bir_lowering=False, num_devices=1)
    arrays, args = {}, []
    shape = inputs["x"].shape
    for name in _INS:
        a = _np.ascontiguousarray(inputs[name])
        if name == "x":
            a = a.reshape(shape[0], shape[1], shape[2] * shape[3])
        arrays[f"in_{name}_dram"] = a
        args.append(nc.dram_tensor(f"in_{name}_dram", a.shape, _mybir.dt.from_np(a.dtype), kind="ExternalInput").ap())
    flat = (shape[0], shape[1], shape[2] * shape[3])
    args.append(nc.dram_tensor("out_dram", flat, _mybir.dt.float32, kind="ExternalOutput").ap())
    attention_block(nc, *args)
    r = _run(nc, [arrays], core_ids=[0])
    return r.results[0]["out_dram"].reshape(shape)
```
